# Optimizing a Trainium2 kernel written in Bass

```python
import numpy as np
import jax
import jax.numpy as jnp

def _softmax(x, axis=-1):
    return jax.nn.softmax(x, axis=axis)

def _gelu(x):
    return jax.nn.gelu(x, approximate=True)

def _silu(x):
    return jax.nn.silu(x)

def _sigmoid(x):
    return jax.nn.sigmoid(x)

def _layernorm(x, axis=-1, eps=1e-05):
    m = jnp.mean(x, axis=axis, keepdims=True)
    v = jnp.var(x, axis=axis, keepdims=True)
    return (x - m) / jnp.sqrt(v + eps)

def _scatter_add(tgt, idx, src, axis=0):
    return tgt.at[idx].add(src)

def _segment_sum(src, seg, n):
    return jax.ops.segment_sum(src, seg, n)
kernel_name = 'mk_adj_preln_d1_adj_r2_ccc0b9'

def setup_inputs(seed: int=0):
    np.random.seed(seed)
    _w = jnp.asarray

    def _rec_inputs():
        import jax
        import jax.numpy as jnp
        _gk = jax.random.key(seed)
        x = -0.0002928 + 1 * jax.random.normal(jax.random.fold_in(_gk, 1), (8192, 256), jnp.float32)
        _a = jax.random.bernoulli(jax.random.fold_in(_gk, 2), 0.00195312, (8192, 8192))
        _a = jnp.logical_or(_a, jnp.eye(8192, dtype=bool))
        _af = _a.astype(jnp.float32)
        adj = _af
        return (x, adj)
    x, adj = _rec_inputs()

    def _L0_gnn_setup():
        import jax, jax.numpy as jnp
        import numpy as np
        N = 4096
        F_IN = 256
        F_OUT = 256
        DENSITY = 0.01
        key = jax.random.key(seed)
        k_x, k_adj, k_w, k_b = jax.random.split(key, 4)
        input_features = jax.random.normal(k_x, (N, F_IN), dtype=jnp.float32)
        adj = (jax.random.uniform(k_adj, (N, N)) < DENSITY).astype(jnp.float32)
        idx = jnp.arange(N)
        adj = adj.at[idx, idx].set(1.0)
        W = jax.random.normal(k_w, (F_IN, F_OUT), dtype=jnp.float32) / np.sqrt(F_IN)
        b = jax.random.normal(k_b, (F_OUT,), dtype=jnp.float32) * 0.01
        return {'input_features': input_features, 'adj': adj, 'W': W, 'b': b}
    _L0_gnn_all = _L0_gnn_setup()
    _L0_gnn_in = {k: v for k, v in _L0_gnn_all.items() if k in ('W', 'b')}
    del _L0_gnn_all
    return {'x': x, 'adj': adj, 'L0_gnn_W': _L0_gnn_in['W'], 'L0_gnn_b': _L0_gnn_in['b']}

def reference(x, adj, L0_gnn_W, L0_gnn_b):
    import jax
    import jax.numpy as jnp

    def _L0_gnn_ref(input_features, adj, W, b):
        import jax, jax.numpy as jnp
        import numpy as np
        N = 4096
        F_IN = 256
        F_OUT = 256
        DENSITY = 0.01
        A = (adj != 0).astype(input_features.dtype)
        hidden = input_features @ W + b
        deg = jnp.sum(A, axis=0)
        return A @ hidden / deg[:, None]
    h = jnp.maximum(_layernorm(x, axis=-1), 0.0)
    x = x + _L0_gnn_ref(h, adj, L0_gnn_W, L0_gnn_b)
    return x

_drawn_inputs = setup_inputs


def setup_inputs(seed=0):
    import zlib

    import numpy as np

    out = dict(_drawn_inputs(seed))
    spreads = {}
    factors = {'L0_gnn_b': 6.034}
    for name, (base, spread) in spreads.items():
        noise = np.random.default_rng([zlib.crc32(name.encode()), seed]).standard_normal(out[name].shape)
        drawn = base * np.exp(spread * noise) if base else spread * noise
        out[name] = jnp.asarray(drawn.astype(out[name].dtype))
    for name, factor in factors.items():
        out[name] = (out[name] * factor).astype(out[name].dtype)
    return out
```

```python
from contextlib import ExitStack

import numpy as np
import concourse.bass as bass
from concourse import mybir


FP32 = mybir.dt.float32
FP16 = mybir.dt.float16
FP8 = mybir.dt.float8e5
I32 = mybir.dt.int32
U32 = mybir.dt.uint32
U16 = mybir.dt.uint16
U8 = mybir.dt.uint8
ALU = mybir.AluOpType
ACT = mybir.ActivationFunctionType
AX = mybir.AxisListType

P = 128
QUADS = 4
QP = P // QUADS
MASK_INT = 4
MASK_FP8 = 2.0 ** -14
LN_EPS = 1e-5
FP16_TOP = 2.0 ** 14


def gnn_kernel(nc, x, adj, w, b, out):
    N, F = x.shape
    TILES = N // P
    QUARTER = N // QUADS
    CHUNKS = 4
    RUN = QUARTER // CHUNKS
    BLOCKS = RUN // P
    LANES = 4
    GROUPS = N // P
    CG = GROUPS // CHUNKS
    PAIRS = GROUPS // 2
    CP = PAIRS // CHUNKS
    FH = F // P
    SLOTS = 2 * CHUNKS
    BODIES = TILES // 2
    SEG = 4
    SEGS = BODIES // SEG
    assert 2 * SEG * QUADS * MASK_INT < 256
    XB = 4
    BATCHES = TILES // XB
    XSLOTS = 2 * CHUNKS

    ctx = ExitStack()
    with ctx:
        def sb(name, shape, dt):
            return ctx.enter_context(nc.sbuf_tensor(name, shape, dt))

        def pb(name):
            return ctx.enter_context(nc.psum_tensor(name, [P, 512], FP32))

        def sem(name):
            return ctx.enter_context(nc.semaphore(name))

        h_parts = sb("h_parts", [P, GROUPS, 2 * F], FP16)
        acc = sb("acc", [P, TILES * F], FP32)
        xs = acc[:, :].rearrange("p (g f) -> p g f", f=F)
        adj_in = sb("adj_in", [P, CHUNKS, 4 * RUN], FP32)
        mask = sb("mask", [P, 2, 4 * RUN], U8)
        maskT = sb("maskT", [P, SLOTS, 4 * RUN], FP8)
        counts = sb("counts", [P, CHUNKS, 4 * RUN], U8)
        spare = sb("spare", [P, CHUNKS * 2 * RUN // 4], FP32)
        half = spare[:, :].bitcast(U8).rearrange("p (k n) -> p k n", k=CHUNKS)
        col_sum = sb("col_sum", [P, QUARTER], FP16)
        rel = spare[:, :].rearrange("p (u g f) -> p u g f", u=2, g=2)
        hs = maskT[:, SLOTS - 3:SLOTS, :].bitcast(FP32)
        low = sb("low", [P, 2, F], FP32)
        w_sb = sb("w_sb", [P, FH, F], FP32)
        b_all = sb("b_all", [P, F], FP32)
        b_col = sb("b_col", [P, FH], FP32)
        w_top = sb("w_top", [P, FH], FP32)
        bound = sb("bound", [P, FH], FP32)
        pow2 = sb("pow2", [P, FH], FP32)
        scale = sb("scale", [P, FH], FP32)
        unscale_all = sb("unscale_all", [P, F], FP32)
        ident = sb("ident", [P, P], FP32)
        ones = sb("ones", [P, P], FP32)
        diag = low[:, :, :].rearrange("p i (h m) -> p i h m", h=FH)
        quad = sb("quad", [P, QUADS], FP16)
        stats = sb("stats", [P, CG, 6], FP32)
        mv = sb("mv", [P, GROUPS, 2], FP32)
        veps = sb("veps", [P, CG], FP32)
        rvar = sb("rvar", [P, CG], FP32)
        root = sb("root", [P, CG], FP32)
        newt = sb("newt", [P, 2, CG], FP32)
        rstd = sb("rstd", [P, GROUPS], FP32)
        rdeg = sb("rdeg", [P, TILES], FP32)
        deg_q = sb("deg_q", [P, TILES], FP32)

        ps_x = [pb("ps_x0"), pb("ps_x1")]
        ps_h = [pb("ps_h0"), pb("ps_h1")]
        ps_y = [pb("ps_y0"), pb("ps_y1")]
        ps_m = pb("ps_m")

        s_adj = [sem(f"adj_loaded{c}") for c in range(CHUNKS)]
        s_x = [sem(f"x_loaded{c}") for c in range(CHUNKS)]
        s_w = sem("w_loaded")
        s_bias = sem("bias_loaded")
        s_const = sem("constants_made")
        s_ident = sem("ident_zeroed")
        s_wT = sem("w_transposed")
        s_scale_step = sem("scale_step")
        s_bcast = sem("scales_broadcast")
        s_ws = sem("weights_scaled")
        s_ln = sem("layernorm_step")
        s_rvar = sem("inverse_variance_ready")
        s_root = sem("root_ready")
        s_xn = sem("pair_normalized")
        s_xT = sem("pair_transposed")
        s_relu = sem("pair_relu_done")
        s_hid = sem("pair_hidden_in_psum")
        s_hs = sem("pair_hidden_in_sbuf")
        s_hi = sem("pair_value_written")
        s_lo = sem("pair_remainder_written")
        s_mask = sem("mask_made")
        s_maskT = sem("mask_transposed")
        s_count = sem("counts_added")
        s_flush = sem("flush_step")
        s_zero = sem("counts_zeroed")
        s_used = sem("maskT_used")
        s_low = sem("low_copied")
        s_acc = sem("tile_added")
        s_unscaled = sem("tile_unscaled")
        s_sums = sem("column_sums_ready")
        s_deg = sem("degrees_in_psum")
        s_rdeg = sem("degree_step")
        s_xl = [sem(f"x_again{s}") for s in range(XSLOTS)]
        s_fin = sem("batch_final")
        s_out = sem("out_stored")

        block = ctx.enter_context(nc.Block())

        adj_v = adj.rearrange("(t c r) (q k n) -> q k r t c n", c=4, r=QP, q=QUADS, k=CHUNKS)
        x_v = x.rearrange("(q b w l) f -> q w b (l f)", q=QUADS, w=QP, l=LANES)
        xs_v = acc[:, :].rearrange("p (b n) -> p b n", n=LANES * F)
        x_rows = x.rearrange("(t p) f -> p t f", p=P)
        out_rows = out.rearrange("(t p) f -> p t f", p=P)
        x_again = adj_in[:, :, :].rearrange("p k (h t f) -> p (k h) t f", h=2, f=F)

        def stationary(slot, blk, lane):
            return maskT[:, slot, :].rearrange("p (b m l) -> p b m l", b=BLOCKS, l=LANES)[:, blk, :, lane]

        @block.sync
        def _(sp):
            def load_adj(tile, chunk):
                for q in range(QUADS):
                    sp.dma_start(adj_in[QP * q:QP * q + QP, chunk, :].rearrange("r (c n) -> r c n", c=4),
                                 adj_v[q, chunk, :, bass.ds(tile, 1), :, :].rearrange("r t c n -> r (t c) n"))\
                      .then_inc(s_adj[chunk], 16)

            for k in range(CHUNKS):
                for q in range(QUADS):
                    sp.dma_start(xs_v[QP * q:QP * q + QP, BLOCKS * k:BLOCKS * (k + 1), :],
                                 x_v[q, :, BLOCKS * k:BLOCKS * (k + 1), :]).then_inc(s_x[k], 16)
                if k > 0:
                    load_adj(0, k - 1)
            load_adj(0, CHUNKS - 1)
            with sp.Fori(1, TILES) as tile:
                for k in range(CHUNKS):
                    sp.wait_ge(s_mask, tile * CHUNKS + (k + 1 - CHUNKS))
                    load_adj(tile, k)

            def load_x(n):
                sp.dma_start(x_again[:, n % XSLOTS, :, :], x_rows[:, XB * n:XB * (n + 1), :])\
                  .then_inc(s_xl[n % XSLOTS], 16)

            for n in range(XSLOTS):
                if n % 2 == 0:
                    sp.wait_ge(s_mask, (TILES - 1) * CHUNKS + n // 2 + 1)
                load_x(n)
            for n in range(BATCHES):
                sp.wait_ge(s_fin, n + 1)
                sp.dma_start(out_rows[:, XB * n:XB * (n + 1), :],
                             xs[:, XB * n:XB * (n + 1), :]).then_inc(s_out, 16)
                if n + XSLOTS < BATCHES:
                    load_x(n + XSLOTS)
            sp.wait_ge(s_out, 16 * BATCHES)

        @block.gpsimd
        def _(pool):
            nc.gpsimd.memset(ident[:, :], 0.0).then_inc(s_ident, 1)
            pool.wait_ge(s_ident, 1)
            nc.gpsimd.affine_select(out=ident[:, :], in_=ident[:, :], compare_op=ALU.not_equal, fill=1.0,
                                    base=0, pattern=[[-1, P]], channel_multiplier=1).then_inc(s_const, 1)
            nc.gpsimd.memset(ones[:, :], 1.0).then_inc(s_const, 1)
            for u in range(PAIRS):
                pool.wait_ge(s_hi, u + 1)
                nc.gpsimd.tensor_tensor(
                    h_parts[:, 2 * u:2 * u + 2, F:2 * F],
                    hs[:, u % 3, :].rearrange("p (g f) -> p g f", g=2),
                    h_parts[:, 2 * u:2 * u + 2, 0:F], ALU.subtract).then_inc(s_lo, 1)
            with pool.Fori(0, TILES) as tile:
                pool.wait_ge(s_acc, tile + 1)
                nc.gpsimd.tensor_tensor(acc[:, bass.ds(tile * F, F)], acc[:, bass.ds(tile * F, F)],
                                        unscale_all[:, :], ALU.mult).then_inc(s_unscaled, 1)

        @block.scalar
        def _(act):
            act.dma_start(w_sb[:, :, :], w.rearrange("(h p) f -> p h f", p=P)).then_inc(s_w, 16)
            act.dma_start(b_all[:, :], b.rearrange("(o f) -> o f", o=1).broadcast_to([P, F]))\
               .then_inc(s_bias, 16)
            act.dma_start(b_col[:, :], b.rearrange("(h p) -> p h", p=P),
                          allow_slow_non_contiguous=True).then_inc(s_bias, 16)

            def value(u):
                act.wait_ge(s_hs, u + 1)
                nc.scalar.activation(h_parts[:, 2 * u:2 * u + 2, 0:F],
                                     hs[:, u % 3, :].rearrange("p (g f) -> p g f", g=2),
                                     ACT.Copy).then_inc(s_hi, 1)

            for k in range(CHUNKS):
                act.wait_ge(s_rvar, k + 1)
                nc.scalar.activation(root[:, :], rvar[:, :], ACT.Sqrt).then_inc(s_root, 1)
                for u in range(k * CP, (k + 1) * CP):
                    act.wait_ge(s_xT, u + 1)
                    if u >= 2:
                        act.wait_ge(s_hid, u - 1)
                    nc.scalar.activation(rel[:, u % 2, :, :], ps_x[u % 2][:, :].rearrange("p (g f) -> p g f", g=2),
                                         ACT.Relu).then_inc(s_relu, 1)
                    if u > k * CP:
                        value(u - 1)
                value((k + 1) * CP - 1)

            def copy_low(tile, bank, first):
                act.wait_ge(s_used, tile * CHUNKS + CHUNKS)
                if not first:
                    act.wait_ge(s_acc, tile - 1)
                nc.scalar.activation(low[:, bank, :], ps_y[bank][:, F:2 * F], ACT.Copy).then_inc(s_low, 1)

            for bank in range(2):
                copy_low(bank, bank, True)
            with act.Fori(1, BODIES) as body:
                for bank in range(2):
                    copy_low(body * 2 + bank, bank, False)

        @block.vector
        def _(dve):
            nc.vector.memset(quad[:, :], 0.0).then_inc(s_scale_step, 1)
            dve.wait_ge(s_scale_step, 1)
            for q in range(QUADS):
                nc.vector.memset(quad[QP * q:QP * (q + 1), q:q + 1], 1.0)
            nc.vector.memset(col_sum[:, :], 0.0)
            nc.vector.memset(counts[:, :, :].bitcast(U32), 0).then_inc(s_zero, 1)

            scale_steps = [1]

            def scale_step(ins):
                scale_steps[0] += 1
                ins.then_inc(s_scale_step, 1)
                dve.wait_ge(s_scale_step, scale_steps[0])

            dve.wait_ge(s_bias, 32)
            nc.vector.scalar_tensor_tensor(out=bound[:, :], in0=b_col[:, :], scalar=-1.0, in1=b_col[:, :],
                                           op0=ALU.mult, op1=ALU.max)
            dve.wait_ge(s_wT, 1)
            scale_step(nc.vector.tensor_reduce(w_top[:, :], ps_x[0][:, :].rearrange("p (h k) -> p h k", h=FH),
                                               AX.X, ALU.max, apply_absolute_value=True))
            scale_step(nc.vector.scalar_tensor_tensor(out=bound[:, :], in0=w_top[:, :], scalar=float(F),
                                                      in1=bound[:, :], op0=ALU.mult, op1=ALU.add))
            scale_step(nc.vector.tensor_scalar(bound[:, :], bound[:, :], 2.0 ** -100, None, ALU.max))
            scale_step(nc.vector.tensor_scalar(pow2[:, :].bitcast(I32), bound[:, :].bitcast(I32), 0x7F800000, None,
                                               ALU.bitwise_and))
            scale_step(nc.vector.reciprocal(scale[:, :], pow2[:, :]))
            scale_step(nc.vector.tensor_scalar(scale[:, :], scale[:, :], FP16_TOP, None, ALU.mult))
            dve.wait_ge(s_const, 1)
            for h in range(FH):
                nc.vector.tensor_scalar(diag[:, 0, h, :], ident[:, :], scale[:, h:h + 1], None, ALU.mult)
                last = nc.vector.tensor_scalar(diag[:, 1, h, :], ident[:, :], pow2[:, h:h + 1], None, ALU.mult)
            scale_step(last)
            dve.wait_ge(s_bcast, 1)
            for h in range(FH):
                nc.vector.tensor_tensor(w_sb[:, h, :], w_sb[:, h, :], ps_m[:, 0:F], ALU.mult)
            nc.vector.tensor_tensor(b_all[:, :], b_all[:, :], ps_m[:, 0:F], ALU.mult)
            assert FP16_TOP * MASK_FP8 == 1.0
            nc.vector.tensor_copy(unscale_all[:, :], ps_m[:, F:2 * F]).then_inc(s_ws, 1)

            ln_steps = [0]

            def ln_step(ins):
                ln_steps[0] += 1
                ins.then_inc(s_ln, 1)
                dve.wait_ge(s_ln, ln_steps[0])

            def statistics(g):
                return nc.vector.bn_stats(stats[:, g % CG, :], xs[:, g, :])

            def normalize(k):
                for g in range(CG):
                    last = nc.vector.bn_aggr(mv[:, k * CG + g, :], stats[:, g, :])
                ln_step(last)
                ln_step(nc.vector.tensor_scalar(veps[:, :], mv[:, k * CG:(k + 1) * CG, 1], LN_EPS, None, ALU.add))
                nc.vector.reciprocal(rvar[:, :], veps[:, :]).then_inc(s_rvar, 1)
                dve.wait_ge(s_root, k + 1)
                ln_step(nc.vector.tensor_tensor(newt[:, 0, :], root[:, :], root[:, :], ALU.mult))
                ln_step(nc.vector.tensor_tensor(newt[:, 1, :], newt[:, 0, :], veps[:, :], ALU.mult))
                ln_step(nc.vector.tensor_scalar(newt[:, 0, :], newt[:, 1, :], -0.5, 1.5, ALU.mult, ALU.add))
                ln_step(nc.vector.tensor_tensor(rstd[:, k * CG:(k + 1) * CG], root[:, :], newt[:, 0, :], ALU.mult))
                for g in range(k * CG, (k + 1) * CG):
                    last = nc.vector.tensor_scalar(xs[:, g, :], xs[:, g, :], mv[:, g, 0:1], rstd[:, g:g + 1],
                                                   ALU.subtract, ALU.mult)
                    if g % 2 == 1:
                        last.then_inc(s_xn, 1)

            def add_bias(u):
                dve.wait_ge(s_hid, u + 1)
                if u >= 3:
                    dve.wait_ge(s_lo, u - 2)
                nc.vector.tensor_tensor(hs[:, u % 3, :].rearrange("p (g f) -> p g f", g=2),
                                        ps_h[u % 2][:, :].rearrange("p (g f) -> p g f", g=2),
                                        b_all[:, None, :].broadcast_to([P, 2, F]), ALU.add).then_inc(s_hs, 1)

            def make_mask(tile, parity, k, refill):
                n = tile * CHUNKS + k
                m = k % 2
                dve.wait_ge(s_adj[k], tile * (16 * QUADS) + 16 * QUADS)
                nc.vector.tensor_scalar(mask[:, m, :], adj_in[:, k, :], 0.0, float(MASK_INT),
                                        ALU.not_equal, ALU.mult).then_inc(s_mask, 1)
                dve.wait_ge(s_mask, n + 1)
                if refill:
                    dve.wait_ge(s_used, n + 1 - SLOTS)
                nc.vector.transpose(
                    maskT[:, parity * CHUNKS + k, :].bitcast(U32).rearrange("p (b c r) -> p b c r", b=BLOCKS, c=4),
                    mask[:, m, :].bitcast(U32).rearrange("p (c b w) -> p b c w", c=4, b=BLOCKS))\
                  .then_inc(s_maskT, 1)
                nc.vector.tensor_tensor(counts[:, k, :].bitcast(U16), counts[:, k, :].bitcast(U16),
                                        mask[:, m, :].bitcast(U16), ALU.add).then_inc(s_count, 1)

            def add_low(tile, bank):
                dve.wait_ge(s_low, tile + 1)
                nc.vector.tensor_tensor(acc[:, bass.ds(tile * F, F)], ps_y[bank][:, 0:F], low[:, bank, :],
                                        ALU.add).then_inc(s_acc, 1)

            def flush(seg, last):
                c16 = counts[:, :, :].bitcast(U16)
                h16 = half[:, :, :].bitcast(U16)
                dve.wait_ge(s_count, (seg + 1) * (2 * SEG * CHUNKS))
                nc.vector.tensor_tensor(h16, c16[:, :, 0:RUN], c16[:, :, RUN:2 * RUN], ALU.add).then_inc(s_flush, 1)
                dve.wait_ge(s_flush, seg * 3 + 1)
                nc.vector.tensor_tensor(h16[:, :, 0:RUN // 2], h16[:, :, 0:RUN // 2], h16[:, :, RUN // 2:RUN],
                                        ALU.add).then_inc(s_flush, 1)
                if not last:
                    nc.vector.memset(counts[:, :, :].bitcast(U32), 0).then_inc(s_zero, 1)
                dve.wait_ge(s_flush, seg * 3 + 2)
                nc.vector.tensor_tensor(col_sum[:, :].rearrange("p (k n) -> p k n", k=CHUNKS),
                                        col_sum[:, :].rearrange("p (k n) -> p k n", k=CHUNKS),
                                        half[:, :, 0:RUN], ALU.add).then_inc(s_flush, 1)

            def body_steps(body):
                for parity in range(2):
                    for k in range(CHUNKS):
                        make_mask(body * 2 + parity, parity, k, True)
                    add_low(body * 2 + (parity - 2), parity)

            for k in range(CHUNKS):
                if k == 0:
                    dve.wait_ge(s_x[0], 16 * QUADS)
                    for g in range(CG):
                        last = statistics(g)
                    ln_step(last)
                normalize(k)
                if k > 0:
                    make_mask(0, 0, k - 1, False)
                if k + 1 < CHUNKS:
                    dve.wait_ge(s_x[k + 1], 16 * QUADS)
                for u in range(k * CP, (k + 1) * CP):
                    if k + 1 < CHUNKS:
                        statistics(2 * (u + CP))
                        last = statistics(2 * (u + CP) + 1)
                    add_bias(u)
                if k + 1 < CHUNKS:
                    ln_step(last)
            make_mask(0, 0, CHUNKS - 1, False)
            dve.wait_ge(s_lo, PAIRS)
            for k in range(CHUNKS):
                make_mask(1, 1, k, False)

            with dve.Fori(1, SEG) as body:
                body_steps(body)
            flush(0, False)
            with dve.Fori(1, SEGS - 1) as seg:
                with dve.Fori(0, SEG) as r:
                    body_steps(seg * SEG + r)
                flush(seg, False)
            with dve.Fori((SEGS - 1) * SEG, BODIES) as body:
                body_steps(body)
            flush(SEGS - 1, True)
            nc.vector.drain().then_inc(s_sums, 1)

            dve.wait_ge(s_deg, 1)
            nc.vector.tensor_scalar(deg_q[:, :].rearrange("p (q b) -> p b q", q=QUADS),
                                    ps_m[:, 0:TILES].rearrange("p (b q) -> p b q", q=QUADS),
                                    1.0 / MASK_INT, None, ALU.mult).then_inc(s_rdeg, 1)
            dve.wait_ge(s_rdeg, 1)
            nc.vector.reciprocal(rdeg[:, :], deg_q[:, :]).then_inc(s_rdeg, 1)
            dve.wait_ge(s_rdeg, 2)
            for n in range(BATCHES):
                if n == BATCHES - 1:
                    add_low(TILES - 2, 0)
                    add_low(TILES - 1, 1)
                dve.wait_ge(s_xl[n % XSLOTS], 16 * (n // XSLOTS + 1))
                dve.wait_ge(s_unscaled, XB * (n + 1))
                for t in range(XB):
                    tile = XB * n + t
                    last = nc.vector.scalar_tensor_tensor(
                        out=xs[:, tile, :], in0=xs[:, tile, :], scalar=rdeg[:, tile:tile + 1],
                        in1=x_again[:, n % XSLOTS, t, :], op0=ALU.mult, op1=ALU.add)
                last.then_inc(s_fin, 1)

        @block.tensor
        def _(pe):
            pe.wait_ge(s_const, 1)
            pe.wait_ge(s_w, 16)
            for fh in range(FH):
                for kh in range(FH):
                    last = nc.tensor.transpose(ps_x[0][:, (fh * FH + kh) * P:(fh * FH + kh + 1) * P],
                                               w_sb[:, kh, fh * P:(fh + 1) * P], ident[:, :])
            last.then_inc(s_wT, 1)
            pe.wait_ge(s_const, 2)
            pe.wait_ge(s_scale_step, 8)
            for i in range(2):
                for h in range(FH):
                    last = nc.tensor.matmul(ps_m[:, (i * FH + h) * P:(i * FH + h + 1) * P], ones[:, :],
                                            diag[:, i, h, :], start=True, stop=True)
            last.then_inc(s_bcast, 1)

            def transpose_pair(u):
                pe.wait_ge(s_xn, u + 1)
                if u >= 2:
                    pe.wait_ge(s_relu, u - 1)
                for g in range(2):
                    for h in range(FH):
                        last = nc.tensor.transpose(ps_x[u % 2][:, (g * FH + h) * P:(g * FH + h + 1) * P],
                                                   xs[:, 2 * u + g, h * P:(h + 1) * P], ident[:, :])
                last.then_inc(s_xT, 1)

            def multiply_pair(u):
                pe.wait_ge(s_relu, u + 1)
                if u == 0:
                    pe.wait_ge(s_ws, 1)
                if u >= 2:
                    pe.wait_ge(s_hs, u - 1)
                for g in range(2):
                    for h in range(FH):
                        last = nc.tensor.matmul(ps_h[u % 2][:, g * F:(g + 1) * F],
                                                rel[:, u % 2, g, h * P:(h + 1) * P], w_sb[:, h, :],
                                                start=(h == 0), stop=(h == FH - 1))
                last.then_inc(s_hid, 1)

            def hidden(k):
                for u in range(k * CP, (k + 1) * CP):
                    transpose_pair(u)
                    if u > k * CP:
                        multiply_pair(u - 1)
                multiply_pair((k + 1) * CP - 1)

            def multiply_chunk(tile, parity, k, reuse):
                pe.wait_ge(s_maskT, tile * CHUNKS + (k + 1))
                if k == 0 and reuse:
                    pe.wait_ge(s_acc, tile - 1)
                nc.tensor.nop(nofuse=True)
                for blk in range(BLOCKS):
                    for lane in range(LANES):
                        g = (k * BLOCKS + blk) * LANES + lane
                        last = nc.tensor.matmul(ps_y[parity][:, :], stationary(parity * CHUNKS + k, blk, lane),
                                                h_parts[:, g, :], start=(g == 0), stop=(g == GROUPS - 1))
                last.then_inc(s_used, 1)

            hidden(0)
            for k in range(1, CHUNKS):
                hidden(k)
                pe.wait_ge(s_lo, k * CP)
                multiply_chunk(0, 0, k - 1, False)
            pe.wait_ge(s_lo, PAIRS)
            multiply_chunk(0, 0, CHUNKS - 1, False)
            for k in range(CHUNKS):
                multiply_chunk(1, 1, k, False)
            with pe.Fori(1, BODIES - 1) as body:
                for parity in range(2):
                    for k in range(CHUNKS):
                        multiply_chunk(body * 2 + parity, parity, k, True)
            for k in range(CHUNKS):
                if k == CHUNKS - 1:
                    pe.wait_ge(s_sums, 1)
                    for blk in range(QUARTER // P):
                        last = nc.tensor.matmul(ps_m[:, QUADS * blk:QUADS * (blk + 1)],
                                                col_sum[:, blk * P:(blk + 1) * P], quad[:, :],
                                                start=True, stop=True)
                    last.then_inc(s_deg, 1)
                multiply_chunk(TILES - 2, 0, k, True)
            for k in range(CHUNKS):
                multiply_chunk(TILES - 1, 1, k, True)


_INS = ["x", "adj", "L0_gnn_W", "L0_gnn_b"]


def kernel(**inputs):
    import concourse.bacc as bacc
    from concourse.bass_utils import run_bass_kernel_spmd

    nc = bacc.Bacc("TRN2", target_bir_lowering=False, num_devices=1)
    arrays, args = {}, []
    for name in _INS:
        a = np.ascontiguousarray(inputs[name])
        arrays[f"in_{name}_dram"] = a
        args.append(nc.dram_tensor(f"in_{name}_dram", a.shape, mybir.dt.from_np(a.dtype), kind="ExternalInput").ap())
    out = nc.dram_tensor("out_0_dram", inputs["x"].shape, FP32, kind="ExternalOutput").ap()
    gnn_kernel(nc, *args, out)
    r = run_bass_kernel_spmd(nc, [arrays], core_ids=[0])
    return r.results[0]["out_0_dram"]
```

```python
from contextlib import ExitStack

import numpy as np
import concourse.bass as bass
from concourse import mybir


FP32 = mybir.dt.float32
FP16 = mybir.dt.float16
FP8 = mybir.dt.float8e5
I32 = mybir.dt.int32
U32 = mybir.dt.uint32
U16 = mybir.dt.uint16
U8 = mybir.dt.uint8
ALU = mybir.AluOpType
ACT = mybir.ActivationFunctionType
AX = mybir.AxisListType

P = 128
QUADS = 4
QP = P // QUADS
MASK_INT = 4
MASK_FP8 = 2.0 ** -14
LN_EPS = 1e-5
FP16_TOP = 2.0 ** 14


def gnn_kernel(nc, x, adj, w, b, out):
    N, F = x.shape
    TILES = N // P
    QUARTER = N // QUADS
    CHUNKS = 4
    RUN = QUARTER // CHUNKS
    BLOCKS = RUN // P
    LANES = 4
    GROUPS = N // P
    CG = GROUPS // CHUNKS
    PAIRS = GROUPS // 2
    CP = PAIRS // CHUNKS
    FH = F // P
    SLOTS = 2 * CHUNKS
    BODIES = TILES // 2
    SEG = 4
    SEGS = BODIES // SEG
    assert 2 * SEG * QUADS * MASK_INT < 256
    XB = 4
    BATCHES = TILES // XB
    ADJ_X = 2 * CHUNKS
    UNITS = GROUPS // LANES
    LOADS = [(0, 1), (1, 1), (2, 2), (4, 4), (8, 4), (12, 4)]
    assert LOADS[-1][0] + LOADS[-1][1] == UNITS and LANES == 4

    ctx = ExitStack()
    with ctx:
        def sb(name, shape, dt):
            return ctx.enter_context(nc.sbuf_tensor(name, shape, dt))

        def pb(name):
            return ctx.enter_context(nc.psum_tensor(name, [P, 512], FP32))

        def sem(name):
            return ctx.enter_context(nc.semaphore(name))

        h_parts = sb("h_parts", [P, GROUPS, 2 * F], FP16)
        acc = sb("acc", [P, TILES * F], FP32)
        xs = acc[:, :].rearrange("p (g f) -> p g f", f=F)
        adj_in = sb("adj_in", [P, CHUNKS, 4 * RUN], FP32)
        mask = sb("mask", [P, 2, 4 * RUN], U8)
        maskT = sb("maskT", [P, SLOTS, 4 * RUN], FP8)
        counts = sb("counts", [P, CHUNKS, 4 * RUN], U8)
        spare = sb("spare", [P, CHUNKS * 2 * RUN // 4], FP32)
        half = spare[:, :].bitcast(U8).rearrange("p (k n) -> p k n", k=CHUNKS)
        col_sum = sb("col_sum", [P, QUARTER], FP16)
        rel = spare[:, :].rearrange("p (u g f) -> p u g f", u=2, g=2)
        hs = maskT[:, SLOTS - 3:SLOTS, :].bitcast(FP32)
        low = sb("low", [P, 2, F], FP32)
        w_sb = sb("w_sb", [P, FH, F], FP32)
        b_all = sb("b_all", [P, F], FP32)
        b_col = sb("b_col", [P, FH], FP32)
        w_top = sb("w_top", [P, FH], FP32)
        bound = sb("bound", [P, FH], FP32)
        pow2 = sb("pow2", [P, FH], FP32)
        scale = sb("scale", [P, FH], FP32)
        unscale_all = sb("unscale_all", [P, F], FP32)
        ident = sb("ident", [P, P], FP32)
        ones = sb("ones", [P, P], FP32)
        diag = low[:, :, :].rearrange("p i (h m) -> p i h m", h=FH)
        quad = sb("quad", [P, QUADS], FP16)
        stats = sb("stats", [P, 2 * LANES, 6], FP32)
        mv = sb("mv", [P, GROUPS, 2], FP32)
        veps = sb("veps", [P, GROUPS], FP32)
        rvar = sb("rvar", [P, GROUPS], FP32)
        root = sb("root", [P, GROUPS], FP32)
        newt = sb("newt", [P, 3, LANES], FP32)
        rstd = sb("rstd", [P, GROUPS], FP32)
        shift = sb("shift", [P, GROUPS], FP32)
        rdeg = sb("rdeg", [P, TILES], FP32)
        deg_q = sb("deg_q", [P, TILES], FP32)

        ps_x = [pb("ps_x0"), pb("ps_x1")]
        ps_h = [pb("ps_h0"), pb("ps_h1")]
        ps_y = [pb("ps_y0"), pb("ps_y1")]
        ps_m = pb("ps_m")

        s_adj = [sem(f"adj_loaded{c}") for c in range(CHUNKS)]
        s_x = [sem(f"x_loaded{n}") for n in range(len(LOADS))]
        s_w = sem("w_loaded")
        s_bias = sem("bias_loaded")
        s_const = sem("constants_made")
        s_ident = sem("ident_zeroed")
        s_wT = sem("w_transposed")
        s_scale_step = sem("scale_step")
        s_bcast = sem("scales_broadcast")
        s_ws = sem("weights_scaled")
        s_ln = sem("layernorm_step")
        s_rvar = sem("inverse_variance_ready")
        s_root = sem("root_ready")
        s_rstd = sem("rstd_ready")
        s_stats = sem("unit_statistics")
        s_xn0 = sem("first_group_normalized")
        s_xn = sem("pair_normalized")
        s_xT = sem("pair_transposed")
        s_relu = sem("pair_relu_done")
        s_hid = sem("pair_hidden_in_psum")
        s_hs = sem("pair_hidden_in_sbuf")
        s_hi = sem("pair_value_written")
        s_lo = sem("pair_remainder_written")
        s_mask = sem("mask_made")
        s_maskT = sem("mask_transposed")
        s_count = sem("counts_added")
        s_flush = sem("flush_step")
        s_zero = sem("counts_zeroed")
        s_used = sem("maskT_used")
        s_low = sem("low_copied")
        s_acc = sem("tile_added")
        s_unscaled = sem("tile_unscaled")
        s_sums = sem("column_sums_ready")
        s_deg = sem("degrees_in_psum")
        s_rdeg = sem("degree_step")
        s_xl = [sem(f"x_again{n}") for n in range(BATCHES)]
        s_fin = sem("batch_final")
        s_out = sem("out_stored")

        block = ctx.enter_context(nc.Block())

        adj_v = adj.rearrange("(t c r) (q k n) -> q k r t c n", c=4, r=QP, q=QUADS, k=CHUNKS)
        x_v = x.rearrange("(q b w l) f -> q w b (l f)", q=QUADS, w=QP, l=LANES)
        xs_v = acc[:, :].rearrange("p (b n) -> p b n", n=LANES * F)
        x_rows = x.rearrange("(t p) f -> p t f", p=P)
        out_rows = out.rearrange("(t p) f -> p t f", p=P)

        def x_again(n):
            if n < ADJ_X:
                at = adj_in[:, n // 2, :][:, (n % 2) * XB * F:(n % 2 + 1) * XB * F]
            elif n < ADJ_X + 2:
                at = counts[:, 2 * (n - ADJ_X):2 * (n - ADJ_X) + 2, :].bitcast(FP32).rearrange("p k n -> p (k n)")
            elif n == ADJ_X + 2:
                at = mask[:, :, :].bitcast(FP32).rearrange("p k n -> p (k n)")
            elif n == ADJ_X + 3:
                at = spare[:, :]
            elif n < ADJ_X + 6:
                at = maskT[:, 2 * (n - ADJ_X - 4):2 * (n - ADJ_X - 4) + 2, :].bitcast(FP32)\
                    .rearrange("p k n -> p (k n)")
            else:
                return x_again(n - ADJ_X - 6)
            return at.rearrange("p (t f) -> p t f", f=F)

        def stationary(slot, blk, lane):
            return maskT[:, slot, :].rearrange("p (b m l) -> p b m l", b=BLOCKS, l=LANES)[:, blk, :, lane]

        @block.sync
        def _(sp):
            def load_adj(tile, chunk):
                for q in range(QUADS):
                    sp.dma_start(adj_in[QP * q:QP * q + QP, chunk, :].rearrange("r (c n) -> r c n", c=4),
                                 adj_v[q, chunk, :, bass.ds(tile, 1), :, :].rearrange("r t c n -> r (t c) n"))\
                      .then_inc(s_adj[chunk], 16)

            for n, (b0, nb) in enumerate(LOADS):
                for q in range(QUADS):
                    sp.dma_start(xs_v[QP * q:QP * q + QP, b0:b0 + nb, :],
                                 x_v[q, :, b0:b0 + nb, :]).then_inc(s_x[n], 16)
                if n >= 3:
                    load_adj(0, n - 3)
            load_adj(0, CHUNKS - 1)
            with sp.Fori(1, TILES) as tile:
                for k in range(CHUNKS):
                    sp.wait_ge(s_mask, tile * CHUNKS + (k + 1 - CHUNKS))
                    load_adj(tile, k)

            def load_x(n):
                sp.dma_start(x_again(n), x_rows[:, XB * n:XB * (n + 1), :]).then_inc(s_xl[n], 16)

            for n in range(ADJ_X):
                if n % 2 == 0:
                    sp.wait_ge(s_mask, (TILES - 1) * CHUNKS + n // 2 + 1)
                load_x(n)
            sp.wait_ge(s_sums, 1)
            for n in range(ADJ_X, ADJ_X + 4):
                load_x(n)
            for n in range(BATCHES):
                if n in (1, 2):
                    sp.wait_ge(s_used, (TILES - 2) * CHUNKS + 2 * n)
                    load_x(ADJ_X + 3 + n)
                sp.wait_ge(s_fin, n + 1)
                sp.dma_start(out_rows[:, XB * n:XB * (n + 1), :],
                             xs[:, XB * n:XB * (n + 1), :]).then_inc(s_out, 16)
                if n + ADJ_X + 6 < BATCHES:
                    load_x(n + ADJ_X + 6)
            sp.wait_ge(s_out, 16 * BATCHES)

        @block.gpsimd
        def _(pool):
            nc.gpsimd.memset(ident[:, :], 0.0).then_inc(s_ident, 1)
            pool.wait_ge(s_ident, 1)
            nc.gpsimd.affine_select(out=ident[:, :], in_=ident[:, :], compare_op=ALU.not_equal, fill=1.0,
                                    base=0, pattern=[[-1, P]], channel_multiplier=1).then_inc(s_const, 1)
            nc.gpsimd.memset(ones[:, :], 1.0).then_inc(s_const, 1)
            nc.gpsimd.memset(counts[:, :, :].bitcast(U32), 0)
            nc.gpsimd.memset(col_sum[:, :], 0.0).then_inc(s_zero, 1)

            def remainder(u):
                pool.wait_ge(s_hi, u + 1)
                nc.gpsimd.tensor_tensor(h_parts[:, 2 * u:2 * u + 2, F:2 * F],
                                        hs[:, u % 3, :].rearrange("p (g f) -> p g f", g=2),
                                        h_parts[:, 2 * u:2 * u + 2, 0:F], ALU.subtract).then_inc(s_lo, 1)

            for u in range(PAIRS):
                remainder(u)

            with pool.Fori(0, TILES) as tile:
                pool.wait_ge(s_acc, tile + 1)
                nc.gpsimd.tensor_tensor(acc[:, bass.ds(tile * F, F)], acc[:, bass.ds(tile * F, F)],
                                        unscale_all[:, :], ALU.mult).then_inc(s_unscaled, 1)

        @block.scalar
        def _(act):
            act.dma_start(w_sb[:, :, :], w.rearrange("(h p) f -> p h f", p=P)).then_inc(s_w, 16)
            act.dma_start(b_all[:, :], b.rearrange("(o f) -> o f", o=1).broadcast_to([P, F]))\
               .then_inc(s_bias, 16)
            act.dma_start(b_col[:, :], b.rearrange("(h p) -> p h", p=P),
                          allow_slow_non_contiguous=True).then_inc(s_bias, 16)

            def take_root(m):
                act.wait_ge(s_rvar, m + 1)
                nc.scalar.activation(root[:, LANES * m:LANES * (m + 1)], rvar[:, LANES * m:LANES * (m + 1)],
                                     ACT.Sqrt).then_inc(s_root, 1)

            def normalize(u):
                if u % 2 == 0:
                    act.wait_ge(s_rstd, u // 2 + 1)
                for g in (2 * u, 2 * u + 1):
                    if g % LANES:
                        last = nc.scalar.activation(xs[:, g, :], xs[:, g, :], ACT.Identity,
                                                    bias=shift[:, g:g + 1], scale=rstd[:, g:g + 1])
                last.then_inc(s_xn, 1)

            def rectify(u):
                act.wait_ge(s_xT, u + 1)
                if u >= 2:
                    act.wait_ge(s_hid, u - 1)
                nc.scalar.activation(rel[:, u % 2, :, :], ps_x[u % 2][:, :].rearrange("p (g f) -> p g f", g=2),
                                     ACT.Relu).then_inc(s_relu, 1)

            def value(u):
                act.wait_ge(s_hs, u + 1)
                nc.scalar.activation(h_parts[:, 2 * u:2 * u + 2, 0:F],
                                     hs[:, u % 3, :].rearrange("p (g f) -> p g f", g=2),
                                     ACT.Copy).then_inc(s_hi, 1)

            take_root(0)
            normalize(0)
            normalize(1)
            for m in range(UNITS):
                rectify(2 * m)
                if m + 1 < UNITS:
                    take_root(m + 1)
                if m > 0:
                    value(2 * m - 1)
                rectify(2 * m + 1)
                if m + 1 < UNITS:
                    normalize(2 * m + 2)
                value(2 * m)
                if m + 1 < UNITS:
                    normalize(2 * m + 3)
            value(PAIRS - 1)

            def copy_low(tile, bank, first):
                act.wait_ge(s_used, tile * CHUNKS + CHUNKS)
                if not first:
                    act.wait_ge(s_acc, tile - 1)
                nc.scalar.activation(low[:, bank, :], ps_y[bank][:, F:2 * F], ACT.Copy).then_inc(s_low, 1)

            for bank in range(2):
                copy_low(bank, bank, True)
            with act.Fori(1, BODIES) as body:
                for bank in range(2):
                    copy_low(body * 2 + bank, bank, False)

        @block.vector
        def _(dve):
            nc.vector.memset(quad[:, :], 0.0).then_inc(s_scale_step, 1)
            dve.wait_ge(s_scale_step, 1)
            for q in range(QUADS):
                nc.vector.memset(quad[QP * q:QP * (q + 1), q:q + 1], 1.0)

            scale_steps = [1]

            def scale_step(ins):
                scale_steps[0] += 1
                ins.then_inc(s_scale_step, 1)
                dve.wait_ge(s_scale_step, scale_steps[0])

            def bound_columns():
                dve.wait_ge(s_bias, 32)
                nc.vector.scalar_tensor_tensor(out=bound[:, :], in0=b_col[:, :], scalar=-1.0, in1=b_col[:, :],
                                               op0=ALU.mult, op1=ALU.max)
                dve.wait_ge(s_wT, 1)
                scale_step(nc.vector.tensor_reduce(w_top[:, :], ps_x[0][:, :].rearrange("p (h k) -> p h k", h=FH),
                                                   AX.X, ALU.max, apply_absolute_value=True))
                scale_step(nc.vector.scalar_tensor_tensor(out=bound[:, :], in0=w_top[:, :], scalar=float(F),
                                                          in1=bound[:, :], op0=ALU.mult, op1=ALU.add))
                scale_step(nc.vector.tensor_scalar(bound[:, :], bound[:, :], 2.0 ** -100, None, ALU.max))
                scale_step(nc.vector.tensor_scalar(pow2[:, :].bitcast(I32), bound[:, :].bitcast(I32), 0x7F800000, None,
                                                   ALU.bitwise_and))
                scale_step(nc.vector.reciprocal(scale[:, :], pow2[:, :]))
                scale_step(nc.vector.tensor_scalar(scale[:, :], scale[:, :], FP16_TOP, None, ALU.mult))
                dve.wait_ge(s_const, 1)
                for h in range(FH):
                    nc.vector.tensor_scalar(diag[:, 0, h, :], ident[:, :], scale[:, h:h + 1], None, ALU.mult)
                    last = nc.vector.tensor_scalar(diag[:, 1, h, :], ident[:, :], pow2[:, h:h + 1], None, ALU.mult)
                scale_step(last)

            def scale_weights():
                dve.wait_ge(s_bcast, 1)
                for h in range(FH):
                    nc.vector.tensor_tensor(w_sb[:, h, :], w_sb[:, h, :], ps_m[:, 0:F], ALU.mult)
                nc.vector.tensor_tensor(b_all[:, :], b_all[:, :], ps_m[:, 0:F], ALU.mult)
                assert FP16_TOP * MASK_FP8 == 1.0
                nc.vector.tensor_copy(unscale_all[:, :], ps_m[:, F:2 * F]).then_inc(s_ws, 1)

            ln_steps = [0]

            def ln_step(ins):
                ln_steps[0] += 1
                ins.then_inc(s_ln, 1)

            def ln_wait():
                dve.wait_ge(s_ln, ln_steps[0])

            def statistics(m, i):
                if i == 0:
                    for n, (m0, _) in enumerate(LOADS):
                        if m == m0:
                            dve.wait_ge(s_x[n], 16 * QUADS)
                ins = nc.vector.bn_stats(stats[:, LANES * (m % 2) + i, :], xs[:, LANES * m + i, :])
                if i == LANES - 1:
                    ins.then_inc(s_stats, 1)

            def aggregate(m):
                dve.wait_ge(s_stats, m + 1)
                for i in range(LANES):
                    last = nc.vector.bn_aggr(mv[:, LANES * m + i, :], stats[:, LANES * (m % 2) + i, :])
                ln_step(last)

            def rows(t, m):
                return t[:, LANES * m:LANES * (m + 1)]

            def add_eps(m):
                ln_wait()
                ln_step(nc.vector.tensor_scalar(rows(veps, m), mv[:, LANES * m:LANES * (m + 1), 1], LN_EPS, None,
                                                ALU.add))

            def invert(m):
                ln_wait()
                nc.vector.reciprocal(rows(rvar, m), rows(veps, m)).then_inc(s_rvar, 1)

            def newton_square(m):
                dve.wait_ge(s_root, m + 1)
                ln_step(nc.vector.tensor_tensor(newt[:, 0, :], rows(root, m), rows(root, m), ALU.mult))

            def newton_times(m):
                ln_wait()
                ln_step(nc.vector.tensor_tensor(newt[:, 1, :], newt[:, 0, :], rows(veps, m), ALU.mult))

            def newton_factor(m):
                ln_wait()
                ln_step(nc.vector.tensor_scalar(newt[:, 2, :], newt[:, 1, :], -0.5, 1.5, ALU.mult, ALU.add))

            def newton_end(m):
                ln_wait()
                ln_step(nc.vector.tensor_tensor(rows(rstd, m), rows(root, m), newt[:, 2, :], ALU.mult))

            def shift_by(m):
                ln_wait()
                nc.vector.scalar_tensor_tensor(out=rows(shift, m), in0=mv[:, LANES * m:LANES * (m + 1), 0],
                                               scalar=-1.0, in1=rows(rstd, m),
                                               op0=ALU.mult, op1=ALU.mult).then_inc(s_rstd, 1)

            def normalize_first(m):
                g = LANES * m
                nc.vector.tensor_scalar(xs[:, g, :], xs[:, g, :], mv[:, g, 0:1], rstd[:, g:g + 1],
                                        ALU.subtract, ALU.mult).then_inc(s_xn0, 1)

            def add_bias(u):
                dve.wait_ge(s_hid, u + 1)
                if u >= 3:
                    dve.wait_ge(s_lo, u - 2)
                nc.vector.tensor_tensor(hs[:, u % 3, :].rearrange("p (g f) -> p g f", g=2),
                                        ps_h[u % 2][:, :].rearrange("p (g f) -> p g f", g=2),
                                        b_all[:, None, :].broadcast_to([P, 2, F]), ALU.add).then_inc(s_hs, 1)

            def make_mask(tile, k):
                dve.wait_ge(s_adj[k], tile * (16 * QUADS) + 16 * QUADS)
                nc.vector.tensor_scalar(mask[:, k % 2, :], adj_in[:, k, :], 0.0, float(MASK_INT),
                                        ALU.not_equal, ALU.mult).then_inc(s_mask, 1)

            def transpose_mask(tile, parity, k, refill):
                dve.wait_ge(s_mask, tile * CHUNKS + (k + 1))
                if refill:
                    dve.wait_ge(s_used, tile * CHUNKS + (k + 1 - SLOTS))
                nc.vector.transpose(
                    maskT[:, parity * CHUNKS + k, :].bitcast(U32).rearrange("p (b c r) -> p b c r", b=BLOCKS, c=4),
                    mask[:, k % 2, :].bitcast(U32).rearrange("p (c b w) -> p b c w", c=4, b=BLOCKS))\
                  .then_inc(s_maskT, 1)

            def count_mask(k):
                nc.vector.tensor_tensor(counts[:, k, :].bitcast(U16), counts[:, k, :].bitcast(U16),
                                        mask[:, k % 2, :].bitcast(U16), ALU.add).then_inc(s_count, 1)

            def do_chunk(tile, parity, k, refill):
                make_mask(tile, k)
                transpose_mask(tile, parity, k, refill)
                count_mask(k)

            def add_low(tile, bank):
                dve.wait_ge(s_low, tile + 1)
                nc.vector.tensor_tensor(acc[:, bass.ds(tile * F, F)], ps_y[bank][:, 0:F], low[:, bank, :],
                                        ALU.add).then_inc(s_acc, 1)

            def flush(seg, last):
                c16 = counts[:, :, :].bitcast(U16)
                h16 = half[:, :, :].bitcast(U16)
                dve.wait_ge(s_count, (seg + 1) * (2 * SEG * CHUNKS))
                nc.vector.tensor_tensor(h16, c16[:, :, 0:RUN], c16[:, :, RUN:2 * RUN], ALU.add).then_inc(s_flush, 1)
                dve.wait_ge(s_flush, seg * 3 + 1)
                nc.vector.tensor_tensor(h16[:, :, 0:RUN // 2], h16[:, :, 0:RUN // 2], h16[:, :, RUN // 2:RUN],
                                        ALU.add).then_inc(s_flush, 1)
                if not last:
                    nc.vector.memset(counts[:, :, :].bitcast(U32), 0).then_inc(s_zero, 1)
                dve.wait_ge(s_flush, seg * 3 + 2)
                nc.vector.tensor_tensor(col_sum[:, :].rearrange("p (k n) -> p k n", k=CHUNKS),
                                        col_sum[:, :].rearrange("p (k n) -> p k n", k=CHUNKS),
                                        half[:, :, 0:RUN], ALU.add).then_inc(s_flush, 1)

            def body_steps(body):
                for parity in range(2):
                    for k in range(CHUNKS):
                        do_chunk(body * 2 + parity, parity, k, True)
                    add_low(body * 2 + (parity - 2), parity)

            for i in range(LANES):
                statistics(0, i)
            aggregate(0)
            statistics(1, 0)
            add_eps(0)
            statistics(1, 1)
            invert(0)
            statistics(1, 2)
            statistics(1, 3)
            newton_square(0)
            newton_times(0)
            newton_factor(0)
            newton_end(0)
            shift_by(0)
            normalize_first(0)
            bound_columns()
            for m in range(UNITS):
                ahead, after = m + 1 < UNITS, m + 2 < UNITS
                if ahead:
                    aggregate(m + 1)
                if after:
                    statistics(m + 2, 0)
                if ahead:
                    add_eps(m + 1)
                if after:
                    statistics(m + 2, 1)
                if ahead:
                    invert(m + 1)
                if m == 0:
                    scale_weights()
                    dve.wait_ge(s_zero, 1)
                else:
                    add_bias(2 * m - 1)
                if ahead:
                    newton_square(m + 1)
                if after:
                    statistics(m + 2, 2)
                if ahead:
                    newton_times(m + 1)
                if after:
                    statistics(m + 2, 3)
                if ahead:
                    newton_factor(m + 1)
                    newton_end(m + 1)
                    shift_by(m + 1)
                    normalize_first(m + 1)
                add_bias(2 * m)
                chunk, part = m // BLOCKS, m % BLOCKS
                if chunk > 0 and part == 1:
                    make_mask(0, chunk - 1)
                elif chunk > 0 and part == 2:
                    transpose_mask(0, 0, chunk - 1, False)
                elif chunk > 0 and part == 3:
                    count_mask(chunk - 1)
            add_bias(PAIRS - 1)
            do_chunk(0, 0, CHUNKS - 1, False)
            dve.wait_ge(s_lo, PAIRS)
            for k in range(CHUNKS):
                do_chunk(1, 1, k, False)

            with dve.Fori(1, SEG) as body:
                body_steps(body)
            flush(0, False)
            with dve.Fori(1, SEGS - 1) as seg:
                with dve.Fori(0, SEG) as r:
                    body_steps(seg * SEG + r)
                flush(seg, False)
            with dve.Fori((SEGS - 1) * SEG, BODIES) as body:
                body_steps(body)
            flush(SEGS - 1, True)
            nc.vector.drain().then_inc(s_sums, 1)

            dve.wait_ge(s_deg, 1)
            nc.vector.tensor_scalar(deg_q[:, :].rearrange("p (q b) -> p b q", q=QUADS),
                                    ps_m[:, 0:TILES].rearrange("p (b q) -> p b q", q=QUADS),
                                    1.0 / MASK_INT, None, ALU.mult).then_inc(s_rdeg, 1)
            dve.wait_ge(s_rdeg, 1)
            nc.vector.reciprocal(rdeg[:, :], deg_q[:, :]).then_inc(s_rdeg, 1)
            dve.wait_ge(s_rdeg, 2)
            for n in range(BATCHES):
                if n == BATCHES - 1:
                    add_low(TILES - 2, 0)
                    add_low(TILES - 1, 1)
                dve.wait_ge(s_xl[n], 16)
                dve.wait_ge(s_unscaled, XB * (n + 1))
                for t in range(XB):
                    tile = XB * n + t
                    last = nc.vector.scalar_tensor_tensor(
                        out=xs[:, tile, :], in0=xs[:, tile, :], scalar=rdeg[:, tile:tile + 1],
                        in1=x_again(n)[:, t, :], op0=ALU.mult, op1=ALU.add)
                last.then_inc(s_fin, 1)

        @block.tensor
        def _(pe):
            pe.wait_ge(s_const, 1)
            pe.wait_ge(s_w, 16)
            for fh in range(FH):
                for kh in range(FH):
                    last = nc.tensor.transpose(ps_x[0][:, (fh * FH + kh) * P:(fh * FH + kh + 1) * P],
                                               w_sb[:, kh, fh * P:(fh + 1) * P], ident[:, :])
            last.then_inc(s_wT, 1)
            pe.wait_ge(s_const, 2)
            pe.wait_ge(s_scale_step, 8)
            for i in range(2):
                for h in range(FH):
                    last = nc.tensor.matmul(ps_m[:, (i * FH + h) * P:(i * FH + h + 1) * P], ones[:, :],
                                            diag[:, i, h, :], start=True, stop=True)
            last.then_inc(s_bcast, 1)

            def transpose_pair(u):
                pe.wait_ge(s_xn0, u // 2 + 1)
                pe.wait_ge(s_xn, u + 1)
                if u >= 2:
                    pe.wait_ge(s_relu, u - 1)
                for g in range(2):
                    for h in range(FH):
                        last = nc.tensor.transpose(ps_x[u % 2][:, (g * FH + h) * P:(g * FH + h + 1) * P],
                                                   xs[:, 2 * u + g, h * P:(h + 1) * P], ident[:, :])
                last.then_inc(s_xT, 1)

            def multiply_pair(u):
                pe.wait_ge(s_relu, u + 1)
                if u == 0:
                    pe.wait_ge(s_ws, 1)
                if u >= 2:
                    pe.wait_ge(s_hs, u - 1)
                for g in range(2):
                    for h in range(FH):
                        last = nc.tensor.matmul(ps_h[u % 2][:, g * F:(g + 1) * F],
                                                rel[:, u % 2, g, h * P:(h + 1) * P], w_sb[:, h, :],
                                                start=(h == 0), stop=(h == FH - 1))
                last.then_inc(s_hid, 1)

            def hidden(k):
                for u in range(k * CP, (k + 1) * CP):
                    transpose_pair(u)
                    if u > k * CP:
                        multiply_pair(u - 1)
                multiply_pair((k + 1) * CP - 1)

            def multiply_chunk(tile, parity, k, reuse):
                pe.wait_ge(s_maskT, tile * CHUNKS + (k + 1))
                if k == 0 and reuse:
                    pe.wait_ge(s_acc, tile - 1)
                nc.tensor.nop(nofuse=True)
                for blk in range(BLOCKS):
                    for lane in range(LANES):
                        g = (k * BLOCKS + blk) * LANES + lane
                        last = nc.tensor.matmul(ps_y[parity][:, :], stationary(parity * CHUNKS + k, blk, lane),
                                                h_parts[:, g, :], start=(g == 0), stop=(g == GROUPS - 1))
                last.then_inc(s_used, 1)

            hidden(0)
            for k in range(1, CHUNKS):
                hidden(k)
                pe.wait_ge(s_lo, k * CP)
                multiply_chunk(0, 0, k - 1, False)
            pe.wait_ge(s_lo, PAIRS)
            multiply_chunk(0, 0, CHUNKS - 1, False)
            for k in range(CHUNKS):
                multiply_chunk(1, 1, k, False)
            with pe.Fori(1, BODIES - 1) as body:
                for parity in range(2):
                    for k in range(CHUNKS):
                        multiply_chunk(body * 2 + parity, parity, k, True)
            for k in range(CHUNKS):
                if k == CHUNKS - 2:
                    pe.wait_ge(s_sums, 1)
                    for blk in range(QUARTER // P):
                        last = nc.tensor.matmul(ps_m[:, QUADS * blk:QUADS * (blk + 1)],
                                                col_sum[:, blk * P:(blk + 1) * P], quad[:, :],
                                                start=True, stop=True)
                    last.then_inc(s_deg, 1)
                multiply_chunk(TILES - 2, 0, k, True)
            for k in range(CHUNKS):
                multiply_chunk(TILES - 1, 1, k, True)


_INS = ["x", "adj", "L0_gnn_W", "L0_gnn_b"]


def kernel(**inputs):
    import concourse.bacc as bacc
    from concourse.bass_utils import run_bass_kernel_spmd

    nc = bacc.Bacc("TRN2", target_bir_lowering=False, num_devices=1)
    arrays, args = {}, []
    for name in _INS:
        a = np.ascontiguousarray(inputs[name])
        arrays[f"in_{name}_dram"] = a
        args.append(nc.dram_tensor(f"in_{name}_dram", a.shape, mybir.dt.from_np(a.dtype), kind="ExternalInput").ap())
    out = nc.dram_tensor("out_0_dram", inputs["x"].shape, FP32, kind="ExternalOutput").ap()
    gnn_kernel(nc, *args, out)
    r = run_bass_kernel_spmd(nc, [arrays], core_ids=[0])
    return r.results[0]["out_0_dram"]
```

```python
from contextlib import ExitStack

import numpy as np
import concourse.bass as bass
from concourse import mybir


FP32 = mybir.dt.float32
FP16 = mybir.dt.float16
FP8 = mybir.dt.float8e5
I32 = mybir.dt.int32
U32 = mybir.dt.uint32
U16 = mybir.dt.uint16
U8 = mybir.dt.uint8
ALU = mybir.AluOpType
ACT = mybir.ActivationFunctionType
AX = mybir.AxisListType

P = 128
QUADS = 4
QP = P // QUADS
MASK_INT = 4
MASK_FP8 = 2.0 ** -14
LN_EPS = 1e-5
FP16_TOP = 2.0 ** 14


def gnn_kernel(nc, x, adj, w, b, out):
    N, F = x.shape
    TILES = N // P
    QUARTER = N // QUADS
    CHUNKS = 4
    RUN = QUARTER // CHUNKS
    BLOCKS = RUN // P
    LANES = 4
    GROUPS = N // P
    PAIRS = GROUPS // 2
    CP = PAIRS // CHUNKS
    FH = F // P
    SLOTS = 2 * CHUNKS
    BODIES = TILES // 2
    SEG = 4
    SEGS = BODIES // SEG
    assert (2 * SEG + 1) * 4 * MASK_INT < 256
    XB = 4
    BATCHES = TILES // XB
    ADJ_X = 2 * CHUNKS
    SHARED = 5
    UNITS = GROUPS // LANES
    LOADS = [(0, 1), (1, 1), (2, 2), (4, 4), (8, 4), (12, 4)]
    assert LOADS[-1][0] + LOADS[-1][1] == UNITS and LANES == 4

    ctx = ExitStack()
    with ctx:
        def sb(name, shape, dt):
            return ctx.enter_context(nc.sbuf_tensor(name, shape, dt))

        def pb(name):
            return ctx.enter_context(nc.psum_tensor(name, [P, 512], FP32))

        def sem(name):
            return ctx.enter_context(nc.semaphore(name))

        h_parts = sb("h_parts", [P, GROUPS, 2 * F], FP16)
        acc = sb("acc", [P, TILES * F], FP32)
        xs = acc[:, :].rearrange("p (g f) -> p g f", f=F)
        adj_in = sb("adj_in", [P, CHUNKS, 4 * RUN], FP32)
        mask = sb("mask", [P, 2, 4 * RUN], U8)
        maskT = sb("maskT", [P, SLOTS, 4 * RUN], FP8)
        counts = sb("counts", [P, CHUNKS, RUN], U8)
        halves = sb("halves", [P, 2 * RUN], U8)
        fours = sb("fours", [P, RUN], U8)
        x_wait = sb("x_wait", [P, XB * F], FP32)
        early = sb("early", [P, 2 * XB * F], FP32)
        rel = early[:, 0:4 * F].rearrange("p (u g f) -> p u g f", u=2, g=2)
        w_sb = early[:, 4 * F:4 * F + FH * F].rearrange("p (h f) -> p h f", h=FH)
        b_all = early[:, 6 * F:7 * F]
        ident = early[:, 7 * F:7 * F + P]
        ones = early[:, 7 * F + P:7 * F + 2 * P]
        assert FH == 2 and 2 * P == F
        col_sum = sb("col_sum", [P, QUARTER], FP16)
        hs = maskT[:, SLOTS - 3:SLOTS, :].bitcast(FP32)
        low = sb("low", [P, 2, F], FP32)
        b_col = sb("b_col", [P, FH], FP32)
        w_top = sb("w_top", [P, FH], FP32)
        bound = sb("bound", [P, FH], FP32)
        pow2 = sb("pow2", [P, FH], FP32)
        scale = sb("scale", [P, FH], FP32)
        unscale_all = sb("unscale_all", [P, F], FP32)
        diag = low[:, :, :].rearrange("p i (h m) -> p i h m", h=FH)
        quad = sb("quad", [P, QUADS], FP16)
        stats = sb("stats", [P, 2 * LANES, 6], FP32)
        mv = sb("mv", [P, GROUPS, 2], FP32)
        veps = sb("veps", [P, GROUPS], FP32)
        rvar = sb("rvar", [P, GROUPS], FP32)
        root = sb("root", [P, GROUPS], FP32)
        newt = sb("newt", [P, 3, LANES], FP32)
        rstd = sb("rstd", [P, GROUPS], FP32)
        shift = sb("shift", [P, GROUPS], FP32)
        rdeg = sb("rdeg", [P, TILES], FP32)
        deg_q = sb("deg_q", [P, TILES], FP32)

        ps_x = [pb("ps_x0"), pb("ps_x1")]
        ps_h = [pb("ps_h0"), pb("ps_h1")]
        ps_y = [pb("ps_y0"), pb("ps_y1")]
        ps_m = pb("ps_m")

        s_adj = [sem(f"adj_loaded{c}") for c in range(CHUNKS)]
        s_x = [sem(f"x_loaded{n}") for n in range(len(LOADS))]
        s_w = sem("w_loaded")
        s_bias = sem("bias_loaded")
        s_bcol = sem("bias_column_loaded")
        s_const = sem("constants_made")
        s_ident = sem("ident_zeroed")
        s_wT = sem("w_transposed")
        s_scale_step = sem("scale_step")
        s_pow2 = sem("pow2_diagonals")
        s_bcast = sem("scales_broadcast")
        s_ws = sem("weights_scaled")
        s_ln = sem("layernorm_step")
        s_rvar = sem("inverse_variance_ready")
        s_root = sem("root_ready")
        s_rstd = sem("rstd_ready")
        s_stats = sem("unit_statistics")
        s_xn0 = sem("first_group_normalized")
        s_xn = sem("pair_normalized")
        s_xT = sem("pair_transposed")
        s_relu = sem("pair_relu_done")
        s_hid = sem("pair_hidden_in_psum")
        s_hs = sem("pair_hidden_in_sbuf")
        s_hi = sem("pair_value_written")
        s_lo = sem("pair_remainder_written")
        s_mask = sem("mask_made")
        s_maskT = sem("mask_transposed")
        s_halves = sem("half_sums")
        s_fours = sem("sums_over_c")
        s_count = sem("counts_added")
        s_zero = sem("counts_zeroed")
        s_used = sem("maskT_used")
        s_low = sem("low_copied")
        s_acc = sem("tile_added")
        s_unscaled = sem("tile_unscaled")
        s_sums = sem("column_sums_flushed")
        s_deg = sem("degrees_in_psum")
        s_rdeg = sem("degree_step")
        s_xl = [sem(f"x_again{n}") for n in range(BATCHES)]
        s_fin = sem("batch_final")
        s_scaled4 = sem("fourth_tile_scaled")
        s_fin4 = sem("fourth_tile_final")
        s_out = sem("out_stored")

        block = ctx.enter_context(nc.Block())

        adj_v = adj.rearrange("(t c r) (q k n) -> q k r t c n", c=4, r=QP, q=QUADS, k=CHUNKS)
        x_v = x.rearrange("(q b w l) f -> q w b (l f)", q=QUADS, w=QP, l=LANES)
        xs_v = acc[:, :].rearrange("p (b n) -> p b n", n=LANES * F)
        x_rows = x.rearrange("(t p) f -> p t f", p=P)
        out_rows = out.rearrange("(t p) f -> p t f", p=P)

        def x_again(n):
            if n < ADJ_X:
                at = adj_in[:, n // 2, :][:, (n % 2) * XB * F:(n % 2 + 1) * XB * F]
            elif n < ADJ_X + 2:
                at = early[:, (n - ADJ_X) * XB * F:(n - ADJ_X + 1) * XB * F]
            elif n == ADJ_X + 2:
                at = x_wait[:, :]
            elif n == ADJ_X + 3:
                at = mask[:, :, :].bitcast(FP32).rearrange("p k n -> p (k n)")
            elif n < ADJ_X + 6:
                at = maskT[:, 2 * (n - ADJ_X - 4):2 * (n - ADJ_X - 4) + 2, :].bitcast(FP32)\
                    .rearrange("p k n -> p (k n)")
            else:
                return x_again(n - ADJ_X - 6)
            return at.rearrange("p (t f) -> p t f", f=F)

        def stationary(slot, blk, lane):
            return maskT[:, slot, :].rearrange("p (b m l) -> p b m l", b=BLOCKS, l=LANES)[:, blk, :, lane]

        def load_adj(engine, quads, tile, chunk):
            for q in quads:
                engine.dma_start(adj_in[QP * q:QP * q + QP, chunk, :].rearrange("r (c n) -> r c n", c=4),
                                 adj_v[q, chunk, :, bass.ds(tile, 1), :, :].rearrange("r t c n -> r (t c) n"))\
                  .then_inc(s_adj[chunk], 16)

        @block.sync
        def _(sp):
            for n, (b0, nb) in enumerate(LOADS):
                for q in (0, 2, 1, 3):
                    sp.dma_start(xs_v[QP * q:QP * q + QP, b0:b0 + nb, :],
                                 x_v[q, :, b0:b0 + nb, :]).then_inc(s_x[n], 16)
                if n == 0:
                    sp.dma_start(b_all, b.rearrange("(o f) -> o f", o=1).broadcast_to([P, F])).then_inc(s_bias, 16)
                if n >= 3:
                    load_adj(sp, (0, 2, 1, 3), 0, n - 3)
            load_adj(sp, (0, 2, 1, 3), 0, CHUNKS - 1)

            def load_tiles(first, end, quads):
                with sp.Fori(first, end) as tile:
                    for k in range(CHUNKS):
                        sp.wait_ge(s_mask, tile * CHUNKS + (k + 1 - CHUNKS))
                        load_adj(sp, quads, tile, k)

            def load_x(n):
                sp.dma_start(x_again(n), x_rows[:, XB * n:XB * (n + 1), :]).then_inc(s_xl[n], 16)

            load_tiles(1, SHARED, (0, 2, 1, 3))
            load_tiles(SHARED, 4 * SEG, (0, 1))
            sp.wait_ge(s_hs, PAIRS)
            for n in range(ADJ_X, ADJ_X + 3):
                load_x(n)
            load_tiles(4 * SEG, TILES, (0, 1))
            for n in range(ADJ_X):
                if n % 2 == 0:
                    sp.wait_ge(s_mask, (TILES - 1) * CHUNKS + n // 2 + 1)
                load_x(n)
            sp.wait_ge(s_maskT, TILES * CHUNKS)
            load_x(ADJ_X + 3)
            late = {2: (2, ADJ_X + 4), 6: (4, ADJ_X + 5)}
            for n in range(BATCHES):
                sp.wait_ge(s_fin, n + 1)
                if n < BATCHES - 1:
                    sp.wait_ge(s_fin4, n + 1)
                end = XB * (n + 1) if n < BATCHES - 1 else TILES - 1
                sp.dma_start(out_rows[:, XB * n:end, :], xs[:, XB * n:end, :]).then_inc(s_out, 16)
                if n + ADJ_X + 6 < BATCHES:
                    load_x(n + ADJ_X + 6)
                if n in late:
                    used, batch = late[n]
                    sp.wait_ge(s_used, (TILES - 2) * CHUNKS + used)
                    load_x(batch)
            sp.wait_ge(s_fin, BATCHES + 1)
            sp.dma_start(out_rows[:, TILES - 1:TILES, :], xs[:, TILES - 1:TILES, :]).then_inc(s_out, 16)
            sp.wait_ge(s_out, 16 * (BATCHES + 1))

        @block.gpsimd
        def _(pool):
            nc.gpsimd.memset(ident, 0.0).then_inc(s_ident, 1)
            pool.wait_ge(s_ident, 1)
            nc.gpsimd.affine_select(out=ident, in_=ident, compare_op=ALU.not_equal, fill=1.0,
                                    base=0, pattern=[[-1, P]], channel_multiplier=1).then_inc(s_const, 1)
            nc.gpsimd.memset(ones, 1.0).then_inc(s_const, 1)
            nc.gpsimd.memset(counts[:, :, :].bitcast(U32), 0)
            nc.gpsimd.memset(col_sum[:, :], 0.0).then_inc(s_zero, 1)

            def remainder(u):
                pool.wait_ge(s_hi, u + 1)
                nc.gpsimd.tensor_tensor(h_parts[:, 2 * u:2 * u + 2, F:2 * F],
                                        hs[:, u % 3, :].rearrange("p (g f) -> p g f", g=2),
                                        h_parts[:, 2 * u:2 * u + 2, 0:F], ALU.subtract).then_inc(s_lo, 1)

            for u in range(PAIRS):
                remainder(u)

            with pool.Fori(0, TILES - 2) as tile:
                pool.wait_ge(s_acc, tile + 1)
                nc.gpsimd.tensor_tensor(acc[:, bass.ds(tile * F, F)], acc[:, bass.ds(tile * F, F)],
                                        unscale_all[:, :], ALU.mult).then_inc(s_unscaled, 1)
            for n in range(BATCHES - 1):
                tile = XB * n + XB - 1
                pool.wait_ge(s_xl[n], 16)
                pool.wait_ge(s_scaled4, n + 1)
                nc.gpsimd.tensor_tensor(xs[:, tile, :], xs[:, tile, :], x_again(n)[:, XB - 1, :],
                                        ALU.add).then_inc(s_fin4, 1)

        @block.scalar
        def _(act):
            act.dma_start(w_sb, w.rearrange("(h p) f -> p h f", p=P)).then_inc(s_w, 16)
            act.dma_start(b_col[:, :], b.rearrange("(h p) -> p h", p=P),
                          allow_slow_non_contiguous=True).then_inc(s_bcol, 16)

            def take_root(m):
                act.wait_ge(s_rvar, m + 1)
                nc.scalar.activation(root[:, LANES * m:LANES * (m + 1)], rvar[:, LANES * m:LANES * (m + 1)],
                                     ACT.Sqrt).then_inc(s_root, 1)

            def normalize(u):
                if u % 2 == 0:
                    act.wait_ge(s_rstd, u // 2 + 1)
                for g in (2 * u, 2 * u + 1):
                    if g % LANES:
                        last = nc.scalar.activation(xs[:, g, :], xs[:, g, :], ACT.Identity,
                                                    bias=shift[:, g:g + 1], scale=rstd[:, g:g + 1])
                last.then_inc(s_xn, 1)

            def rectify(u):
                act.wait_ge(s_xT, u + 1)
                if u >= 2:
                    act.wait_ge(s_hid, u - 1)
                nc.scalar.activation(rel[:, u % 2, :, :], ps_x[u % 2][:, :].rearrange("p (g f) -> p g f", g=2),
                                     ACT.Relu).then_inc(s_relu, 1)

            def value(u):
                act.wait_ge(s_hs, u + 1)
                nc.scalar.activation(h_parts[:, 2 * u:2 * u + 2, 0:F],
                                     hs[:, u % 3, :].rearrange("p (g f) -> p g f", g=2),
                                     ACT.Copy).then_inc(s_hi, 1)

            take_root(0)
            act.wait_ge(s_const, 1)
            act.wait_ge(s_scale_step, 6)
            for h in range(FH):
                last = nc.scalar.activation(diag[:, 1, h, :], ident, ACT.Copy, scale=pow2[:, h:h + 1])
            last.then_inc(s_pow2, 1)
            normalize(0)
            normalize(1)
            rectify(0)
            rectify(1)
            take_root(1)
            act.wait_ge(s_bcast, 2)
            assert FP16_TOP * MASK_FP8 == 1.0
            nc.scalar.activation(unscale_all[:, :], ps_y[1][:, 0:F], ACT.Copy)
            for m in range(UNITS):
                if m > 0:
                    rectify(2 * m + 1)
                if m + 1 < UNITS:
                    normalize(2 * m + 2)
                if m > 0:
                    value(2 * m - 1)
                if m + 2 < UNITS:
                    take_root(m + 2)
                if m + 1 < UNITS:
                    normalize(2 * m + 3)
                    rectify(2 * m + 2)
                value(2 * m)
            value(PAIRS - 1)

            def copy_low(tile, bank, first):
                act.wait_ge(s_used, tile * CHUNKS + CHUNKS)
                if not first:
                    act.wait_ge(s_acc, tile - 1)
                nc.scalar.activation(low[:, bank, :], ps_y[bank][:, F:2 * F], ACT.Copy).then_inc(s_low, 1)

            for bank in range(2):
                copy_low(bank, bank, True)

            def load_ahead(tile):
                for k in range(CHUNKS):
                    act.wait_ge(s_mask, tile * CHUNKS + ((SHARED - 2) * CHUNKS + k + 1 - CHUNKS))
                    load_adj(act, (2, 3), tile + (SHARED - 2), k)

            with act.Fori(1, BODIES - 2) as body:
                for bank in range(2):
                    load_ahead(body * 2 + bank)
                    copy_low(body * 2 + bank, bank, False)
            load_ahead(TILES - 4)
            copy_low(TILES - 4, 0, False)
            copy_low(TILES - 3, 1, False)
            act.wait_ge(s_rdeg, 2)
            for n in range(BATCHES - 1):
                if n == (BATCHES - 1) // 2:
                    copy_low(TILES - 2, 0, False)
                tile = XB * n + XB - 1
                act.wait_ge(s_unscaled, tile + 1)
                nc.scalar.activation(xs[:, tile, :], xs[:, tile, :], ACT.Copy,
                                     scale=rdeg[:, tile:tile + 1]).then_inc(s_scaled4, 1)
            copy_low(TILES - 1, 1, False)

        @block.vector
        def _(dve):
            nc.vector.memset(quad[:, :], 0.0).then_inc(s_scale_step, 1)
            dve.wait_ge(s_scale_step, 1)
            for q in range(QUADS):
                nc.vector.memset(quad[QP * q:QP * (q + 1), q:q + 1], 1.0)

            scale_steps = [1]

            def scale_step(ins):
                scale_steps[0] += 1
                ins.then_inc(s_scale_step, 1)

            def scale_wait():
                dve.wait_ge(s_scale_step, scale_steps[0])

            def diagonal(h):
                return nc.vector.tensor_scalar(diag[:, 0, h, :], ident, scale[:, h:h + 1], None, ALU.mult)

            def scale_weights():
                dve.wait_ge(s_bcast, 1)
                for h in range(FH):
                    last = nc.vector.tensor_tensor(w_sb[:, h, :], w_sb[:, h, :], ps_m[:, 0:F], ALU.mult)
                last.then_inc(s_ws, 1)

            def scale_bias():
                dve.wait_ge(s_bias, 16)
                nc.vector.tensor_tensor(b_all, b_all, ps_m[:, 0:F], ALU.mult)

            ln_steps = [0]

            def ln_step(ins):
                ln_steps[0] += 1
                ins.then_inc(s_ln, 1)

            def ln_wait():
                dve.wait_ge(s_ln, ln_steps[0])

            def statistics(m, i):
                if i == 0:
                    for n, (m0, _) in enumerate(LOADS):
                        if m == m0:
                            dve.wait_ge(s_x[n], 16 * QUADS)
                ins = nc.vector.bn_stats(stats[:, LANES * (m % 2) + i, :], xs[:, LANES * m + i, :])
                if i == LANES - 1:
                    ins.then_inc(s_stats, 1)

            def aggregate(m):
                dve.wait_ge(s_stats, m + 1)
                for i in range(LANES):
                    last = nc.vector.bn_aggr(mv[:, LANES * m + i, :], stats[:, LANES * (m % 2) + i, :])
                ln_step(last)

            def rows(t, m):
                return t[:, LANES * m:LANES * (m + 1)]

            def add_eps(m):
                ln_wait()
                ln_step(nc.vector.tensor_scalar(rows(veps, m), mv[:, LANES * m:LANES * (m + 1), 1], LN_EPS, None,
                                                ALU.add))

            def invert(m):
                ln_wait()
                nc.vector.reciprocal(rows(rvar, m), rows(veps, m)).then_inc(s_rvar, 1)

            def newton_square(m):
                dve.wait_ge(s_root, m + 1)
                ln_step(nc.vector.tensor_tensor(newt[:, 0, :], rows(root, m), rows(root, m), ALU.mult))

            def newton_times(m):
                ln_wait()
                ln_step(nc.vector.tensor_tensor(newt[:, 1, :], newt[:, 0, :], rows(veps, m), ALU.mult))

            def newton_factor(m):
                ln_wait()
                ln_step(nc.vector.tensor_scalar(newt[:, 2, :], newt[:, 1, :], -0.5, 1.5, ALU.mult, ALU.add))

            def newton_end(m):
                ln_wait()
                ln_step(nc.vector.tensor_tensor(rows(rstd, m), rows(root, m), newt[:, 2, :], ALU.mult))

            def shift_by(m):
                ln_wait()
                nc.vector.scalar_tensor_tensor(out=rows(shift, m), in0=mv[:, LANES * m:LANES * (m + 1), 0],
                                               scalar=-1.0, in1=rows(rstd, m),
                                               op0=ALU.mult, op1=ALU.mult).then_inc(s_rstd, 1)

            def normalize_first(m):
                g = LANES * m
                nc.vector.tensor_scalar(xs[:, g, :], xs[:, g, :], mv[:, g, 0:1], rstd[:, g:g + 1],
                                        ALU.subtract, ALU.mult).then_inc(s_xn0, 1)

            def add_bias(u):
                dve.wait_ge(s_hid, u + 1)
                if u >= 3:
                    dve.wait_ge(s_lo, u - 2)
                nc.vector.tensor_tensor(hs[:, u % 3, :].rearrange("p (g f) -> p g f", g=2),
                                        ps_h[u % 2][:, :].rearrange("p (g f) -> p g f", g=2),
                                        b_all[:, None, :].broadcast_to([P, 2, F]), ALU.add).then_inc(s_hs, 1)

            def make_mask(tile, k):
                dve.wait_ge(s_adj[k], tile * (16 * QUADS) + 16 * QUADS)
                nc.vector.tensor_scalar(mask[:, k % 2, :], adj_in[:, k, :], 0.0, float(MASK_INT),
                                        ALU.not_equal, ALU.mult).then_inc(s_mask, 1)

            def transpose_mask(tile, parity, k, refill):
                if refill:
                    dve.wait_ge(s_used, tile * CHUNKS + (k + 1 - SLOTS))
                nc.vector.transpose(
                    maskT[:, parity * CHUNKS + k, :].bitcast(U32).rearrange("p (b c r) -> p b c r", b=BLOCKS, c=4),
                    mask[:, k % 2, :].bitcast(U32).rearrange("p (c b w) -> p b c w", c=4, b=BLOCKS))\
                  .then_inc(s_maskT, 1)

            def halve(k):
                m16 = mask[:, k % 2, :].bitcast(U16)
                nc.vector.tensor_tensor(halves[:, :].bitcast(U16), m16[:, 0:RUN], m16[:, RUN:2 * RUN],
                                        ALU.add).then_inc(s_halves, 1)

            def quarter(n):
                h16 = halves[:, :].bitcast(U16)
                dve.wait_ge(s_halves, n + 1)
                nc.vector.tensor_tensor(fours[:, :].bitcast(U16), h16[:, 0:RUN // 2], h16[:, RUN // 2:RUN],
                                        ALU.add).then_inc(s_fours, 1)

            def count(n, k):
                dve.wait_ge(s_fours, n + 1)
                nc.vector.tensor_tensor(counts[:, k, :].bitcast(U16), counts[:, k, :].bitcast(U16),
                                        fours[:, :].bitcast(U16), ALU.add).then_inc(s_count, 1)

            def do_chunk(tile, parity, k, refill, count_before=True):
                make_mask(tile, k)
                if count_before:
                    count(tile * CHUNKS + (k - 1), (k - 1) % CHUNKS)
                dve.wait_ge(s_mask, tile * CHUNKS + (k + 1))
                halve(k)
                transpose_mask(tile, parity, k, refill)
                quarter(tile * CHUNKS + k)

            def add_low(tile, bank):
                dve.wait_ge(s_low, tile + 1)
                nc.vector.tensor_tensor(acc[:, bass.ds(tile * F, F)], ps_y[bank][:, 0:F], low[:, bank, :],
                                        ALU.add).then_inc(s_acc, 1)

            def flush(seg, last):
                dve.wait_ge(s_count, seg * (2 * SEG * CHUNKS) + (2 * SEG * CHUNKS - 1 + last))
                wide = col_sum[:, :].rearrange("p (k n) -> p k n", k=CHUNKS)
                nc.vector.tensor_tensor(wide, wide, counts[:, :, :], ALU.add).then_inc(s_sums, 1)
                if not last:
                    dve.wait_ge(s_sums, seg + 1)
                    nc.vector.memset(counts[:, :, :].bitcast(U32), 0).then_inc(s_zero, 1)
                    dve.wait_ge(s_zero, seg + 2)

            def body_steps(body):
                for parity in range(2):
                    for k in range(CHUNKS):
                        do_chunk(body * 2 + parity, parity, k, True)
                    add_low(body * 2 + (parity - 2), parity)

            dve.wait_ge(s_bcol, 16)
            scale_step(nc.vector.scalar_tensor_tensor(out=bound[:, :], in0=b_col[:, :], scalar=-1.0,
                                                      in1=b_col[:, :], op0=ALU.mult, op1=ALU.max))
            dve.wait_ge(s_wT, 1)
            scale_step(nc.vector.tensor_reduce(w_top[:, :], ps_x[0][:, :].rearrange("p (h k) -> p h k", h=FH),
                                               AX.X, ALU.max, apply_absolute_value=True))
            for i in range(LANES):
                statistics(0, i)
            scale_wait()
            scale_step(nc.vector.scalar_tensor_tensor(out=bound[:, :], in0=w_top[:, :], scalar=float(F),
                                                      in1=bound[:, :], op0=ALU.mult, op1=ALU.add))
            aggregate(0)
            scale_wait()
            scale_step(nc.vector.tensor_scalar(bound[:, :], bound[:, :], 2.0 ** -100, None, ALU.max))
            add_eps(0)
            scale_wait()
            scale_step(nc.vector.tensor_scalar(pow2[:, :].bitcast(I32), bound[:, :].bitcast(I32), 0x7F800000, None,
                                               ALU.bitwise_and))
            invert(0)
            scale_wait()
            scale_step(nc.vector.reciprocal(scale[:, :], pow2[:, :]))
            scale_wait()
            scale_step(nc.vector.tensor_scalar(scale[:, :], scale[:, :], FP16_TOP, None, ALU.mult))
            dve.wait_ge(s_const, 1)
            newton_square(0)
            scale_wait()
            diagonal(0)
            newton_times(0)
            scale_step(diagonal(1))
            newton_factor(0)
            newton_end(0)
            shift_by(0)
            normalize_first(0)
            statistics(1, 0)
            scale_weights()
            for i in range(1, LANES):
                statistics(1, i)
            aggregate(1)
            scale_bias()
            add_eps(1)
            invert(1)
            for m in range(UNITS):
                ahead, after = m + 1 < UNITS, m + 2 < UNITS
                if ahead:
                    newton_square(m + 1)
                if after:
                    statistics(m + 2, 0)
                if ahead:
                    newton_times(m + 1)
                if after:
                    statistics(m + 2, 1)
                if ahead:
                    newton_factor(m + 1)
                if after:
                    statistics(m + 2, 2)
                if ahead:
                    newton_end(m + 1)
                if after:
                    statistics(m + 2, 3)
                if ahead:
                    shift_by(m + 1)
                    normalize_first(m + 1)
                if m == 0:
                    dve.wait_ge(s_zero, 1)
                else:
                    add_bias(2 * m - 1)
                if after:
                    aggregate(m + 2)
                    add_eps(m + 2)
                    invert(m + 2)
                chunk, part = m // BLOCKS, m % BLOCKS
                if chunk >= 2 and part == 0:
                    do_chunk(0, 0, chunk - 1, False)
                add_bias(2 * m)
                if chunk in (1, CHUNKS - 1):
                    k = 0 if chunk == 1 else chunk
                    if part == 1:
                        make_mask(0, k)
                        if k > 0:
                            count(k - 1, k - 1)
                    elif part == 2:
                        dve.wait_ge(s_mask, k + 1)
                        halve(k)
                        transpose_mask(0, 0, k, False)
                    elif part == 3:
                        quarter(k)
            add_bias(PAIRS - 1)
            do_chunk(1, 1, 0, False)
            dve.wait_ge(s_lo, PAIRS)
            for k in range(1, CHUNKS):
                do_chunk(1, 1, k, False)

            with dve.Fori(1, SEG) as body:
                body_steps(body)
            flush(0, False)
            with dve.Fori(1, SEGS - 1) as seg:
                with dve.Fori(0, SEG) as r:
                    body_steps(seg * SEG + r)
                flush(seg, False)
            with dve.Fori((SEGS - 1) * SEG, BODIES - 1) as body:
                body_steps(body)
            for k in range(CHUNKS):
                do_chunk(TILES - 2, 0, k, True)
            add_low(TILES - 4, 0)
            for k in range(CHUNKS):
                n = (TILES - 1) * CHUNKS + k
                if k >= 2:
                    dve.wait_ge(s_maskT, n - 1)
                make_mask(TILES - 1, k)
                count(n - 1, (k - 1) % CHUNKS)
                dve.wait_ge(s_mask, n + 1)
                halve(k)
                if k in range(1, CHUNKS - 1):
                    transpose_mask(TILES - 1, 1, k - 1, True)
                quarter(n)
            count(TILES * CHUNKS - 1, CHUNKS - 1)
            flush(SEGS - 1, True)
            transpose_mask(TILES - 1, 1, CHUNKS - 2, True)
            transpose_mask(TILES - 1, 1, CHUNKS - 1, True)
            add_low(TILES - 3, 1)

            dve.wait_ge(s_deg, 1)
            nc.vector.tensor_scalar(deg_q[:, :].rearrange("p (q b) -> p b q", q=QUADS),
                                    ps_m[:, 0:TILES].rearrange("p (b q) -> p b q", q=QUADS),
                                    1.0 / MASK_INT, None, ALU.mult).then_inc(s_rdeg, 1)
            dve.wait_ge(s_rdeg, 1)
            nc.vector.reciprocal(rdeg[:, :], deg_q[:, :]).then_inc(s_rdeg, 1)
            dve.wait_ge(s_rdeg, 2)

            def finish(tile):
                return nc.vector.scalar_tensor_tensor(
                    out=xs[:, tile, :], in0=xs[:, tile, :], scalar=rdeg[:, tile:tile + 1],
                    in1=x_again(tile // XB)[:, tile % XB, :], op0=ALU.mult, op1=ALU.add)

            def unscale(tile):
                dve.wait_ge(s_acc, tile + 1)
                nc.vector.tensor_tensor(xs[:, tile, :], xs[:, tile, :], unscale_all[:, :], ALU.mult)\
                  .then_inc(s_unscaled, 1)

            for n in range(BATCHES - 1):
                dve.wait_ge(s_xl[n], 16)
                dve.wait_ge(s_unscaled, XB * (n + 1) - 1)
                for t in range(XB - 1):
                    last = finish(XB * n + t)
                last.then_inc(s_fin, 1)
            dve.wait_ge(s_unscaled, TILES - 2)
            add_low(TILES - 2, 0)
            unscale(TILES - 2)
            dve.wait_ge(s_xl[BATCHES - 1], 16)
            finish(TILES - 4)
            finish(TILES - 3)
            dve.wait_ge(s_unscaled, TILES - 1)
            finish(TILES - 2).then_inc(s_fin, 1)
            add_low(TILES - 1, 1)
            unscale(TILES - 1)
            dve.wait_ge(s_unscaled, TILES)
            finish(TILES - 1).then_inc(s_fin, 1)

        @block.tensor
        def _(pe):
            def keep_busy(times):
                for _ in range(times):
                    nc.tensor.transpose(ps_y[0][:, 0:P], ident, ident)

            pe.wait_ge(s_const, 1)
            keep_busy(6)
            pe.wait_ge(s_w, 16)
            for fh in range(FH):
                for kh in range(FH):
                    last = nc.tensor.transpose(ps_x[0][:, (fh * FH + kh) * P:(fh * FH + kh + 1) * P],
                                               w_sb[:, kh, fh * P:(fh + 1) * P], ident)
            last.then_inc(s_wT, 1)
            keep_busy(20)
            pe.wait_ge(s_const, 2)

            def broadcast(i):
                for h in range(FH):
                    last = nc.tensor.matmul((ps_m, ps_y[1])[i][:, h * P:(h + 1) * P], ones,
                                            diag[:, i, h, :], start=True, stop=True)
                last.then_inc(s_bcast, 1)

            pe.wait_ge(s_scale_step, 9)
            broadcast(0)

            def transpose_pair(u):
                pe.wait_ge(s_xn0, u // 2 + 1)
                pe.wait_ge(s_xn, u + 1)
                if u >= 2:
                    pe.wait_ge(s_relu, u - 1)
                for g in range(2):
                    for h in range(FH):
                        last = nc.tensor.transpose(ps_x[u % 2][:, (g * FH + h) * P:(g * FH + h + 1) * P],
                                                   xs[:, 2 * u + g, h * P:(h + 1) * P], ident)
                last.then_inc(s_xT, 1)

            def multiply_pair(u):
                pe.wait_ge(s_relu, u + 1)
                if u == 0:
                    pe.wait_ge(s_ws, 1)
                if u >= 2:
                    pe.wait_ge(s_hs, u - 1)
                for g in range(2):
                    for h in range(FH):
                        last = nc.tensor.matmul(ps_h[u % 2][:, g * F:(g + 1) * F],
                                                rel[:, u % 2, g, h * P:(h + 1) * P], w_sb[:, h, :],
                                                start=(h == 0), stop=(h == FH - 1))
                last.then_inc(s_hid, 1)

            def multiply_chunk(tile, parity, k, reuse):
                pe.wait_ge(s_maskT, tile * CHUNKS + (k + 1))
                if k == 0 and reuse:
                    pe.wait_ge(s_acc, tile - 1)
                nc.tensor.nop(nofuse=True)
                for blk in range(BLOCKS):
                    for lane in range(LANES):
                        g = (k * BLOCKS + blk) * LANES + lane
                        last = nc.tensor.matmul(ps_y[parity][:, :], stationary(parity * CHUNKS + k, blk, lane),
                                                h_parts[:, g, :], start=(g == 0), stop=(g == GROUPS - 1))
                last.then_inc(s_used, 1)

            transpose_pair(0)
            transpose_pair(1)
            multiply_pair(0)
            pe.wait_ge(s_pow2, 1)
            broadcast(1)
            multiply_pair(1)
            transpose_pair(2)
            for u in range(2, PAIRS):
                if u + 1 < PAIRS:
                    transpose_pair(u + 1)
                multiply_pair(u)
                k = (u + 1) // CP
                if (u + 1) % CP == 0 and k > 1:
                    pe.wait_ge(s_lo, (k - 1) * CP)
                    multiply_chunk(0, 0, k - 2, False)
            pe.wait_ge(s_lo, PAIRS)
            multiply_chunk(0, 0, CHUNKS - 1, False)
            for k in range(CHUNKS):
                multiply_chunk(1, 1, k, False)
            with pe.Fori(1, BODIES - 1) as body:
                for parity in range(2):
                    for k in range(CHUNKS):
                        multiply_chunk(body * 2 + parity, parity, k, True)
            pe.wait_ge(s_sums, SEGS)
            for blk in range(QUARTER // P):
                last = nc.tensor.matmul(ps_m[:, QUADS * blk:QUADS * (blk + 1)],
                                        col_sum[:, blk * P:(blk + 1) * P], quad[:, :],
                                        start=True, stop=True)
            last.then_inc(s_deg, 1)
            for parity in range(2):
                for k in range(CHUNKS):
                    multiply_chunk(TILES - 2 + parity, parity, k, True)


_INS = ["x", "adj", "L0_gnn_W", "L0_gnn_b"]


def kernel(**inputs):
    import concourse.bacc as bacc
    from concourse.bass_utils import run_bass_kernel_spmd

    nc = bacc.Bacc("TRN2", target_bir_lowering=False, num_devices=1)
    arrays, args = {}, []
    for name in _INS:
        a = np.ascontiguousarray(inputs[name])
        arrays[f"in_{name}_dram"] = a
        args.append(nc.dram_tensor(f"in_{name}_dram", a.shape, mybir.dt.from_np(a.dtype), kind="ExternalInput").ap())
    out = nc.dram_tensor("out_0_dram", inputs["x"].shape, FP32, kind="ExternalOutput").ap()
    gnn_kernel(nc, *args, out)
    r = run_bass_kernel_spmd(nc, [arrays], core_ids=[0])
    return r.results[0]["out_0_dram"]
```
